# Optimizing a Trainium2 kernel written in Bass

```python
import numpy as np
import jax
import jax.numpy as jnp

def _softmax(x, axis=-1):
    return jax.nn.softmax(x, axis=axis)

def _gelu(x):
    return jax.nn.gelu(x, approximate=True)

def _silu(x):
    return jax.nn.silu(x)

def _sigmoid(x):
    return jax.nn.sigmoid(x)

def _layernorm(x, axis=-1, eps=1e-05):
    m = jnp.mean(x, axis=axis, keepdims=True)
    v = jnp.var(x, axis=axis, keepdims=True)
    return (x - m) / jnp.sqrt(v + eps)

def _scatter_add(tgt, idx, src, axis=0):
    return tgt.at[idx].add(src)

def _segment_sum(src, seg, n):
    return jax.ops.segment_sum(src, seg, n)
kernel_name = 'mk_early_fusion_d1_tok_img768_r4_1ec06c'

def setup_inputs(seed: int=0):
    np.random.seed(seed)
    _w = jnp.asarray

    def _rec_inputs():
        import jax
        import jax.numpy as jnp
        _rk = jax.random.key(seed)
        x = -0.00016672 + 0.999947 * jax.random.normal(jax.random.fold_in(_rk, 1), (32, 3, 224, 224), jnp.float32)
        txt = 0.000193175 + 0.554495 * jax.random.normal(jax.random.fold_in(_rk, 2), (32, 77, 192), jnp.float32)
        return (x, txt)
    x, txt = _rec_inputs()

    def _L0_tok_setup():
        import jax, jax.numpy as jnp
        import numpy as np
        PATCH = 16

        def _patchify(x, p):
            B, C, H, W = x.shape
            Hp, Wp = (H // p, W // p)
            xu = x.reshape(B, C, Hp, p, Wp, p).transpose(0, 1, 2, 4, 3, 5)
            num_patches = Hp * Wp
            return xu.reshape(B, num_patches, -1)
        key = jax.random.key(seed)
        k1, k2, k3 = jax.random.split(key, 3)
        B, C, H = (64, 3, 96)
        hidden = 192
        d = C * PATCH * PATCH
        x = jax.random.normal(k1, (B, C, H, H), dtype=jnp.float32)
        W = jax.random.normal(k2, (hidden, d), dtype=jnp.float32) * 0.02
        b = jax.random.normal(k3, (hidden,), dtype=jnp.float32) * 0.02
        return {'x': x, 'W': W, 'b': b}
    _L0_tok_all = _L0_tok_setup()
    _L0_tok_in = {k: v for k, v in _L0_tok_all.items() if k in ('W', 'b')}
    del _L0_tok_all

    def _L0_attn_setup():
        import jax, jax.numpy as jnp
        import numpy as np
        ALPHA, BETA, GAMMA = (1.9, 3.8, 15.2)
        NUM_HEADS = 12

        def _rp_bucket_euc(height, width, skip):
            coords = np.stack(np.meshgrid(np.arange(height), np.arange(width), indexing='ij'), -1)
            coords = coords.reshape(-1, 2).astype(np.float64)
            diff = coords[:, None, :] - coords[None, :, :]
            dis = np.round(np.sqrt((diff ** 2).sum(-1)))
            log_idx = np.minimum(np.round(ALPHA + np.log(np.maximum(dis, 1e-09) / ALPHA) / np.log(GAMMA / ALPHA) * (BETA - ALPHA)), BETA).astype(np.int64)
            bucket = np.where(dis <= ALPHA, np.round(dis).astype(np.int64), log_idx)
            bucket = bucket - bucket.min()
            nb = 2 * int(BETA) + 1
            if skip > 0:
                L = height * width
                full = np.full((skip + L, skip + L), nb, dtype=np.int64)
                full[skip:, skip:] = bucket
                bucket, nb = (full, nb + 1)
            return (jnp.asarray(bucket), nb)
        key = jax.random.key(seed)
        ks = jax.random.split(key, 4)
        B, N, C = (8, 1025, 192)
        hd = C // NUM_HEADS
        nb = 2 * int(BETA) + 1 + 1
        return {'x': jax.random.normal(ks[0], (B, N, C), jnp.float32), 'qkv_w': jax.random.normal(ks[1], (3 * C, C), jnp.float32) * 0.02, 'proj_w': jax.random.normal(ks[2], (C, C), jnp.float32) * 0.02, 'proj_b': jnp.zeros((C,), jnp.float32), 'rpe_w': jax.random.normal(ks[3], (hd, nb), jnp.float32) * 0.02}
    _L0_attn_all = _L0_attn_setup()
    _L0_attn_in = {k: v for k, v in _L0_attn_all.items() if k in ('qkv_w', 'proj_w', 'proj_b', 'rpe_w')}
    del _L0_attn_all

    def _L0_ffn_setup():
        import jax, jax.numpy as jnp
        import numpy as np
        D_MODEL = 192
        KAN_HIDDEN = 512
        NUM_CP = 16
        DEGREE = 3
        RMIN, RMAX = (-4.0, 4.0)

        def bspline_basis(x, num_cp=NUM_CP, degree=DEGREE, rmin=RMIN, rmax=RMAX):
            h = (rmax - rmin) / (num_cp - degree)
            knots = rmin - degree * h + jnp.arange(num_cp + degree + 1, dtype=x.dtype) * h
            xe = x[..., None]
            b = ((xe >= knots[:-1]) & (xe < knots[1:])).astype(x.dtype)
            for d in range(1, degree + 1):
                t0 = knots[:-(d + 1)]
                t1 = knots[d:-1]
                t2 = knots[d + 1:]
                t3 = knots[1:-d]
                b = (xe - t0) / (t1 - t0) * b[..., :-1] + (t2 - xe) / (t2 - t3) * b[..., 1:]
            return b

        def kan_layer(x, w):
            basis = bspline_basis(x)
            return jnp.einsum('ndk,odk->no', basis, w)
        key = jax.random.key(seed)
        kx, k1, k2 = jax.random.split(key, 3)
        x = jax.random.normal(kx, (2, 512, D_MODEL), dtype=jnp.float32)
        w1 = jax.random.normal(k1, (KAN_HIDDEN, D_MODEL, NUM_CP), dtype=jnp.float32) * (1.0 / np.sqrt(D_MODEL * NUM_CP))
        w2 = jax.random.normal(k2, (D_MODEL, KAN_HIDDEN, NUM_CP), dtype=jnp.float32) * (1.0 / np.sqrt(KAN_HIDDEN * NUM_CP))
        return {'x': x, 'w1': w1, 'w2': w2}
    _L0_ffn_all = _L0_ffn_setup()
    _L0_ffn_in = {k: v for k, v in _L0_ffn_all.items() if k in ('w1', 'w2')}
    del _L0_ffn_all
    return {'x': x, 'txt': txt, 'L0_tok_W': _L0_tok_in['W'], 'L0_tok_b': _L0_tok_in['b'], 'L0_attn_qkv_w': _L0_attn_in['qkv_w'], 'L0_attn_proj_w': _L0_attn_in['proj_w'], 'L0_attn_proj_b': _L0_attn_in['proj_b'], 'L0_attn_rpe_w': _L0_attn_in['rpe_w'], 'L0_ffn_w1': _L0_ffn_in['w1'], 'L0_ffn_w2': _L0_ffn_in['w2']}

def reference(x, txt, L0_tok_W, L0_tok_b, L0_attn_qkv_w, L0_attn_proj_w, L0_attn_proj_b, L0_attn_rpe_w, L0_ffn_w1, L0_ffn_w2):
    import jax
    import jax.numpy as jnp

    def _L0_tok_ref(x, W, b):
        import jax, jax.numpy as jnp
        import numpy as np
        PATCH = 16

        def _patchify(x, p):
            B, C, H, W = x.shape
            Hp, Wp = (H // p, W // p)
            xu = x.reshape(B, C, Hp, p, Wp, p).transpose(0, 1, 2, 4, 3, 5)
            num_patches = Hp * Wp
            return xu.reshape(B, num_patches, -1)
        patches = _patchify(x, PATCH)
        return jnp.einsum('bnd,hd->bnh', patches, W) + b

    def _L0_attn_ref(x, qkv_w, proj_w, proj_b, rpe_w):
        import jax, jax.numpy as jnp
        import numpy as np
        ALPHA, BETA, GAMMA = (1.9, 3.8, 15.2)
        NUM_HEADS = 12

        def _rp_bucket_euc(height, width, skip):
            coords = np.stack(np.meshgrid(np.arange(height), np.arange(width), indexing='ij'), -1)
            coords = coords.reshape(-1, 2).astype(np.float64)
            diff = coords[:, None, :] - coords[None, :, :]
            dis = np.round(np.sqrt((diff ** 2).sum(-1)))
            log_idx = np.minimum(np.round(ALPHA + np.log(np.maximum(dis, 1e-09) / ALPHA) / np.log(GAMMA / ALPHA) * (BETA - ALPHA)), BETA).astype(np.int64)
            bucket = np.where(dis <= ALPHA, np.round(dis).astype(np.int64), log_idx)
            bucket = bucket - bucket.min()
            nb = 2 * int(BETA) + 1
            if skip > 0:
                L = height * width
                full = np.full((skip + L, skip + L), nb, dtype=np.int64)
                full[skip:, skip:] = bucket
                bucket, nb = (full, nb + 1)
            return (jnp.asarray(bucket), nb)
        B, N, C = x.shape
        H = NUM_HEADS
        hd = C // H
        scale = hd ** (-0.5)
        n_modalities = 1
        height = int((N // n_modalities) ** 0.5)
        skip = N - n_modalities * height * height
        rp_bucket, _ = _rp_bucket_euc(height, height, skip)
        qkv = (x @ qkv_w.T).reshape(B, N, 3, H, hd).transpose(2, 0, 3, 1, 4)
        q, k, v = (qkv[0] * scale, qkv[1], qkv[2])
        attn = jnp.einsum('bhid,bhjd->bhij', q, k)
        lookup = jnp.einsum('bhid,dm->bhim', q, rpe_w)
        bias = jnp.take_along_axis(lookup, rp_bucket[None, None, :, :], axis=3)
        attn = jax.nn.softmax(attn + bias, axis=-1)
        out = jnp.einsum('bhij,bhjd->bhid', attn, v)
        out = out.transpose(0, 2, 1, 3).reshape(B, N, C)
        return out @ proj_w.T + proj_b

    def _L0_ffn_ref(x, w1, w2):
        import jax, jax.numpy as jnp
        import numpy as np
        D_MODEL = 192
        KAN_HIDDEN = 512
        NUM_CP = 16
        DEGREE = 3
        RMIN, RMAX = (-4.0, 4.0)

        def bspline_basis(x, num_cp=NUM_CP, degree=DEGREE, rmin=RMIN, rmax=RMAX):
            h = (rmax - rmin) / (num_cp - degree)
            knots = rmin - degree * h + jnp.arange(num_cp + degree + 1, dtype=x.dtype) * h
            xe = x[..., None]
            b = ((xe >= knots[:-1]) & (xe < knots[1:])).astype(x.dtype)
            for d in range(1, degree + 1):
                t0 = knots[:-(d + 1)]
                t1 = knots[d:-1]
                t2 = knots[d + 1:]
                t3 = knots[1:-d]
                b = (xe - t0) / (t1 - t0) * b[..., :-1] + (t2 - xe) / (t2 - t3) * b[..., 1:]
            return b

        def kan_layer(x, w):
            basis = bspline_basis(x)
            return jnp.einsum('ndk,odk->no', basis, w)
        B, T, D = x.shape
        input_dtype = x.dtype
        h = x.reshape(B * T, D).astype(jnp.float32)
        h = kan_layer(h, w1)
        h = kan_layer(h, w2)
        h = h.astype(input_dtype)
        return h.reshape(B, T, -1)
    h = _L0_tok_ref(x, L0_tok_W, L0_tok_b)
    h = jnp.concatenate([h, txt], axis=1)
    h = h + _L0_attn_ref(_layernorm(h, axis=-1), L0_attn_qkv_w, L0_attn_proj_w, L0_attn_proj_b, L0_attn_rpe_w)
    h = h + _L0_ffn_ref(_layernorm(h, axis=-1), L0_ffn_w1, L0_ffn_w2)
    return h

_drawn_inputs = setup_inputs


def setup_inputs(seed=0):
    import zlib

    import numpy as np

    out = dict(_drawn_inputs(seed))
    spreads = {'L0_attn_proj_b': (0.0, 0.1)}
    factors = {'L0_attn_qkv_w': 6.452, 'L0_attn_proj_w': 6.508, 'L0_attn_rpe_w': 8.0}
    for name, (base, spread) in spreads.items():
        noise = np.random.default_rng([zlib.crc32(name.encode()), seed]).standard_normal(out[name].shape)
        drawn = base * np.exp(spread * noise) if base else spread * noise
        out[name] = jnp.asarray(drawn.astype(out[name].dtype))
    for name, factor in factors.items():
        out[name] = (out[name] * factor).astype(out[name].dtype)
    return out
```

```python
from contextlib import ExitStack

import numpy as np

import concourse.bass as bass
from concourse import mybir

F32 = mybir.dt.float32
ALU = mybir.AluOpType
ACT = mybir.ActivationFunctionType
AX_X = mybir.AxisListType.X

P = 128
B = 32
N_IMG = 196
N_TXT = 77
N = N_IMG + N_TXT
C = 192
H = 12
D = C // H
HC = C // 2
KP = 6
GRID = int(N ** 0.5)
NG = GRID * GRID
SKIP = N - NG
TT = 91
NT = N // TT
HID = 512
HB = HID // P
NCP = 16
RADIUS1, RADIUS2 = 1, 3
W1 = (8 + RADIUS1) * GRID
W2 = (8 + RADIUS2) * GRID
NX = N + 4
GW = 2 * N
ATT_TILES = 27
S_BUF = 3
E_BUF = 4
SLOTS = (12, 16, 16)
NSLOT = sum(SLOTS)
SLOT0 = (0, 12, 28)
MAGIC = 1.5 * 2.0 ** 23
H_KNOT = 8.0 / 13.0
XSCALE = 1.0 / (4.0 * H_KNOT)
XBIAS = (4.0 / H_KNOT + 3.0) / 4.0 - 0.5
XLO, XHI = -0.5, 19.0 / 4.0 - 0.5
EPS = 1e-5
QSCALE = D ** -0.5

N_CD, N_CA = 17, 5
N_LN = 9
N_FIX = 3 * 24 + 3


def att_tile(u):
    g, r = divmod(u, 9)
    return (4 * g + r // 2, r % 2) if r < 8 else (g, None)


def fixes_before(u):
    g, r = divmod(u, 9)
    return g * 25 + 3 * r


JOBS = ([("tok", t) for t in range(NT)] + [("yT", t) for t in range(NT)] + [("qk", j) for j in range(4)]
        + [("v", t) for t in range(NT)] + [("oT", t) for t in range(3)] + [("proj", t) for t in range(NT)]
        + [("zT", t) for t in range(NT)])
JOB = {job: j for j, job in enumerate(JOBS)}
EVAC_BY = {"tok": "dve", "yT": "act", "qk": "act", "v": "act", "oT": "act", "proj": "dve", "zT": "act"}


def evac_engine(job):
    if job[0] == "qk" and job[1] >= 2:
        return "dve"
    return EVAC_BY[job[0]]


def evac_count(j):
    e = evac_engine(JOBS[j])
    return e, sum(evac_engine(x) == e for x in JOBS[:j + 1])


N_EVAC = {e: sum(evac_engine(x) == e for x in JOBS) for e in ("act", "dve")}


def plan_front():
    s = [(("tok", t), 2.0) for t in range(NT)] + [(("ln", 0), 5.0)]
    s += [(("yT", t), 0.7) for t in range(NT)] + [(("qk", j), 1.0) for j in range(4)]
    s += [(("v", t), 0.7) for t in range(NT)]
    for u in range(ATT_TILES + 2):
        if u < ATT_TILES:
            s.append((("scores", u), 0.8))
        if 1 <= u <= ATT_TILES:
            s.append((("pT", u - 1), 0.4))
        if u >= 2:
            s.append((("pv", u - 2), 0.8))
    s.append((("norm", 0), 3.0))
    s += [(("oT", t), 0.5) for t in range(3)] + [(("proj", t), 0.7) for t in range(NT)]
    s += [(("ln", 1), 5.0)] + [(("zT", t), 0.5) for t in range(NT)]
    return s


def plan_prep(g):
    order = ["d0", "d1", "d2", "a0", "a1", "a2", "a3", "d3", "d4", "a4", "d5", "d6", "d7", "d8", "d9",
             "d10", "d11", "d12", "d13", "d14", "d15", "d16"]
    return [(("prep", g, o), 0.4) for o in order]


def plan_back():
    s = plan_prep(0)
    s += [(("slot", 0, k), 3.6) for k in range(SLOTS[0])]
    s += [(("hidden", b), 0.5) for b in range(HB)] + plan_prep(1)
    for k in range(SLOTS[1]):
        s.append((("slot", 1, k), 1.8))
        if k == 2:
            s += plan_prep(2)
    s += [(("slot", 2, k), 1.8) for k in range(SLOTS[2])]
    s += [(("ffn_out", 0), 0.5)] + [(("res", t), 0.5) for t in range(NT)]
    return s


def merge(front, back):
    tf, tb = sum(w for _, w in front), sum(w for _, w in back)
    keyed, at = [], 0.0
    for n, (s, w) in enumerate(front):
        keyed.append((at / tf, 1, n, s, "f"))
        at += w
    at = 0.0
    for n, (s, w) in enumerate(back):
        keyed.append((at / tb, 0, n, s, "b"))
        at += w
    return [(side, s) for _, _, _, s, side in sorted(keyed, key=lambda k: k[:3])]


def plan_body(has_front, has_back):
    f = plan_front() if has_front else []
    b = plan_back() if has_back else []
    m = merge(f, b)
    return m + ([("f", ("keep", 0))] if has_front else [])


def build(nc, xT, txt, tok_w, tok_b, wqkv, wproj, proj_b, rpe, w1, w2, ident_in, mask_in, small_in, out):
    with ExitStack() as ctx:
        def sb(name, shape, dt=F32):
            return ctx.enter_context(nc.sbuf_tensor(name, shape, dt))

        def sem(name):
            return ctx.enter_context(nc.semaphore(name))

        w1_sb = sb("w1_sb", [P, 24, HID])
        w2_sb = sb("w2_sb", [P, NCP, HB, C])
        tokw_sb = sb("tokw_sb", [P, KP, C])
        tokb_sb = sb("tokb_sb", [TT, C])
        wqkv_sb = sb("wqkv_sb", [HC, 2, 3 * C])
        wproj_sb = sb("wproj_sb", [HC, 2, C])
        projb_sb = sb("projb_sb", [TT, C])
        rpe_sb = sb("rpe_sb", [HC, 8])
        ident = sb("ident", [P, P])
        masks = sb("masks", [P, 2, W1 + W2])
        small = sb("small", [P, 8])

        x_sb = sb("x_sb", [P, KP, N_IMG])
        h_sb = sb("h_sb", [TT, NT, C])
        hres = sb("hres", [TT, NT, C])
        stats = sb("stats", [TT, NT, 6])
        mv = sb("mv", [TT, NT, 2])
        rstd = sb("rstd", [TT, NT])
        z = sb("z", [TT, NT, 256])
        yT = sb("yT", [HC, 2, N])
        q = sb("q", [HC, 2, 2, N])
        kx = sb("kx", [HC, 2, NX])
        v = sb("v", [TT, NT, H, D + 1])
        probs = sb("probs", [P, S_BUF, N])
        nmax = sb("nmax", [P, S_BUF])
        pT = sb("pT_sb", [TT, 2, 3 * P])
        oC = sb("oC", [32, H, D + 1])
        rs = sb("rs", [P, 2 * H])
        rsC = sb("rsC", [32, H])
        oN = sb("oN", [P, 2 * H, D])
        oNC = sb("oNC", [32, H, D])
        oT = yT

        x1 = sb("x1", [P, GW])
        x2 = sb("x2", [P, HB, N])
        val = sb("val", [P, 2, 4, GW])
        idx = sb("idx", [P, 2, 4, GW])
        g_ = sb("g_", [P, GW])
        ta = sb("ta", [P, GW])
        ty = sb("ty", [P, GW])
        basis = sb("basis", [P, E_BUF, GW])
        yf = sb("yf", [HC, 2, N])
        o_sb = sb("o_sb", [TT, NT, C])

        pf = [ctx.enter_context(nc.psum_tensor(f"pf{b}", [P, 512], F32)) for b in range(HB)]
        ps = [ctx.enter_context(nc.psum_tensor(f"ps{b}", [P, 512], F32)) for b in range(2)]
        pt = ctx.enter_context(nc.psum_tensor("pt", [P, 512], F32))
        po = ctx.enter_context(nc.psum_tensor("po", [P, 512], F32))
        ring = [ps[0], ps[1], pt]
        o_AB = po[:, 0:2 * H * (D + 1)].rearrange("p (h d) -> p h d", d=D + 1)
        o_C = po[0:32, 2 * H * (D + 1):2 * H * (D + 1) + 4 * (D + 1)].rearrange("p (h d) -> p h d", d=D + 1)

        s_const = sem("s_const")
        s_wffn = sem("s_wffn")
        s_ones = sem("s_ones")
        s_x = sem("s_x")
        s_txt = sem("s_txt")
        s_out = sem("s_out")
        s_job = sem("s_job")
        s_evac = {"act": sem("s_evac_act"), "dve": sem("s_evac_dve")}
        s_half = sem("s_half")
        s_ln = sem("s_ln")
        s_var = sem("s_var")
        s_rstd = sem("s_rstd")
        s_hb = sem("s_hb")
        s_dup = sem("s_dup")
        s_keep = sem("s_keep")
        s_score = sem("s_score")
        s_pair = sem("s_pair")
        s_fix = sem("s_fix")
        s_max = sem("s_max")
        s_exp = sem("s_exp")
        s_ptr = sem("s_ptr")
        s_ptc = sem("s_ptc")
        s_pv = sem("s_pv")
        s_oc = sem("s_oc")
        s_rs = sem("s_rs")
        s_on = sem("s_on")
        s_cd = sem("s_cd")
        s_ca = sem("s_ca")
        s_basis = sem("s_basis")
        s_slot = sem("s_slot")
        s_hid = sem("s_hid")
        s_ffn = sem("s_ffn")
        s_rT = sem("s_rT")
        s_res = sem("s_res")

        def wait(eng, s, value):
            if isinstance(value, int) and value <= 0:
                return
            eng.wait_ge(s, value)

        def first(img):
            return isinstance(img, int) and img == 0

        def apart(eng):
            eng.nop(nofuse=True)

        def wait_job(eng, img, j):
            e, n = evac_count(j)
            wait(eng, s_evac[e], img * N_EVAC[e] + n)

        def cols(t):
            return slice(TT * t, TT * t + TT)

        block = ctx.enter_context(nc.Block())

        def run(eng, do_front, do_back):
            def body(i, has_front, has_back):
                for side, step in plan_body(has_front, has_back):
                    if side == "f":
                        do_front(i, step)
                    else:
                        do_back(i - 1, step)
            body(0, True, False)
            body(1, True, True)
            with eng.Fori(2, B) as i:
                body(i, True, True)
            body(B, False, True)

        @block.sync
        def _(eng):
            for dst, src in ((tokw_sb, tok_w), (tokb_sb, tok_b), (wqkv_sb, wqkv), (wproj_sb, wproj),
                             (projb_sb, proj_b), (rpe_sb, rpe), (ident, ident_in), (masks, mask_in), (small, small_in)):
                dst_ap = dst[tuple(slice(None) for _ in dst.shape)]
                eng.dma_start(dst_ap, src).then_inc(s_const, 16)

            def load(i):
                eng.dma_start(x_sb[:, :, :], xT[i]).then_inc(s_x, 16)

            def load_txt(i):
                eng.dma_start(h_sb[TT - N_TXT:TT, 2, :], txt[i]).then_inc(s_txt, 16)

            load(0)
            load_txt(0)
            eng.dma_start(w1_sb[:, :, :], w1).then_inc(s_wffn, 16)
            eng.dma_start(w2_sb[:, :, :, :], w2).then_inc(s_wffn, 16)

            def body(i, has_next, has_back):
                if has_next:
                    eng.wait_ge(s_job, (i - 1) * len(JOBS) + NT)
                    load(i)
                    eng.wait_ge(s_keep, i)
                    load_txt(i)
                if has_back:
                    eng.wait_ge(s_res, (i - 1) * NT)
                    eng.dma_start(out[i - 2].rearrange("(t p) c -> p t c", p=TT), o_sb[:, :, :]).then_inc(s_out, 16)

            body(1, True, False)
            with eng.Fori(2, B) as i:
                body(i, True, True)
            body(B, False, True)
            body(B + 1, False, True)
            eng.wait_ge(s_out, 16 * B)

        @block.tensor
        def _(eng):
            def front(i, step):
                kind, t = step
                if kind in ("tok", "yT", "qk", "v", "oT", "proj", "zT"):
                    j = JOB[step]
                    dst = ring[j % 3]
                    if j >= 3:
                        wait_job(eng, i, j - 3)
                    elif not first(i):
                        wait_job(eng, i - 1, len(JOBS) - 1)
                if kind == "tok":
                    n = TT if t < 2 else N_IMG - 2 * TT
                    if t == 0:
                        eng.wait_ge(s_x, 16 * (i + 1))
                    for c in range(KP):
                        mm = nc.tensor.matmul(dst[0:n, 0:C], x_sb[:, c, TT * t:TT * t + n], tokw_sb[:, c, :],
                                              start=(c == 0), stop=(c == KP - 1))
                    mm.then_inc(s_job, 1)
                elif kind == "yT":
                    eng.wait_ge(s_ln, i * 2 * N_LN + 6 + t + 1)
                    for c in range(2):
                        mm = nc.tensor.transpose(dst[0:HC, TT * c:TT * c + TT], z[:, t, HC * c:HC * c + HC],
                                                 ident[0:TT, 0:TT])
                    mm.then_inc(s_job, 1)
                elif kind == "qk":
                    wait_job(eng, i, JOB[("yT", NT - 1)])
                    for c in range(2):
                        mm = nc.tensor.matmul(dst[0:HC, 0:N], wqkv_sb[:, c, HC * t:HC * t + HC], yT[:, c, :],
                                              start=(c == 0), stop=(c == 1))
                    mm.then_inc(s_job, 1)
                elif kind == "v":
                    for c in range(2):
                        mm = nc.tensor.matmul(dst[0:TT, 0:C], yT[:, c, cols(t)], wqkv_sb[:, c, 2 * C:3 * C],
                                              start=(c == 0), stop=(c == 1))
                    mm.then_inc(s_job, 1)
                elif kind == "scores":
                    u = t
                    if u == 0:
                        for j in range(JOB[("qk", 0)], JOB[("v", NT - 1)] + 1):
                            wait_job(eng, i, j)
                    if u >= 2:
                        eng.wait_ge(s_exp, i * ATT_TILES + u - 1)
                    bank = ps[u % 2]
                    head, ti = att_tile(u)
                    if ti is not None:
                        heads, i0, m, p0 = [head], SKIP + P * ti, P, None
                    else:
                        heads, i0, m = [4 * head + n for n in range(4)], 0, 32
                    if ti is None:
                        apart(eng)
                    for n, hd in enumerate(heads):
                        half, pair, par = hd // 6, (hd % 6) // 2, hd % 2
                        rows = slice(32 * pair, 32 * pair + 32)
                        if ti is None and n == 2:
                            eng.wait_ge(s_pair, i * 3 + head + 1)
                            apart(eng)
                        mm = nc.tensor.matmul(bank[m * n:m * n + m, 0:NX], q[rows, half, par, i0:i0 + m],
                                              kx[rows, half, :], start=True, stop=True)
                        if ti is None and n == 1:
                            mm.then_inc(s_pair, 1)
                    mm.then_inc(s_score, 1)
                elif kind == "pT":
                    u = t
                    eng.wait_ge(s_exp, i * ATT_TILES + u + 1)
                    if u >= 1:
                        eng.wait_ge(s_ptc, i * ATT_TILES + u)
                    for jb in range(3):
                        mm = nc.tensor.transpose(pt[0:TT, P * jb:P * jb + P], probs[:, u % S_BUF, cols(jb)],
                                                 ident[:, :])
                    mm.then_inc(s_ptr, 1)
                elif kind == "pv":
                    u = t
                    eng.wait_ge(s_ptc, i * ATT_TILES + u + 1)
                    if u == 0 and not first(i):
                        eng.wait_ge(s_on, i * 2)
                    g = u // 9
                    if u % 9 == 0 and g > 0:
                        eng.wait_ge(s_oc, i * 3 + g)
                    head, ti = att_tile(u)
                    heads = [head] if ti is not None else [4 * head + n for n in range(4)]
                    for n, hd in enumerate(heads):
                        for jb in range(3):
                            if ti is not None:
                                o = o_AB[:, ti * H + hd, :]
                                lhs = pT[:, u % 2, P * jb:P * jb + P]
                            else:
                                o = o_C[:, n, :]
                                lhs = pT[:, u % 2, P * jb + 32 * n:P * jb + 32 * n + 32]
                            mm = nc.tensor.matmul(o, lhs, v[:, jb, hd, :], start=(jb == 0), stop=(jb == 2))
                    mm.then_inc(s_pv, 1)
                elif kind == "oT":
                    eng.wait_ge(s_on, i * 2 + 2)
                    apart(eng)
                    for c in range(2):
                        if t < 2:
                            src = oN[:, t * H:(t + 1) * H, :].rearrange("p h d -> p (h d)")[:, HC * c:HC * c + HC]
                            mm = nc.tensor.transpose(dst[0:HC, P * c:P * c + P], src, ident[:, :])
                        else:
                            src = oNC[0:SKIP, :, :].rearrange("p h d -> p (h d)")[:, HC * c:HC * c + HC]
                            mm = nc.tensor.transpose(dst[0:HC, P * c:P * c + SKIP], src, ident[0:SKIP, 0:SKIP])
                    mm.then_inc(s_job, 1)
                elif kind == "proj":
                    if t == 0:
                        for m in range(3):
                            wait_job(eng, i, JOB[("oT", m)])
                    for c in range(2):
                        mm = nc.tensor.matmul(dst[0:TT, 0:C], oT[:, c, cols(t)], wproj_sb[:, c, :],
                                              start=(c == 0), stop=(c == 1))
                    mm.then_inc(s_job, 1)
                elif kind == "zT":
                    eng.wait_ge(s_ln, (i * 2 + 1) * N_LN + 6 + t + 1)
                    eng.wait_ge(s_dup, i * NT + t + 1)
                    for c in range(2):
                        mm = nc.tensor.transpose(dst[:, TT * c:TT * c + TT], z[:, t, P * c:P * c + P],
                                                 ident[0:TT, 0:TT])
                    mm.then_inc(s_job, 1)

            def back(i, step):
                kind = step[0]
                if kind == "slot":
                    _, g, k = step
                    n = SLOT0[g] + k
                    eng.wait_ge(s_basis, i * NSLOT + n + 1)
                    e = basis[:, n % E_BUF, :]
                    if g == 0 and k == 0:
                        wait(eng, s_ffn, i * 2)
                        wait(eng, s_res, i * NT)
                    if g == 1 and k == 0:
                        eng.wait_ge(s_hid, i * HB + 2)
                    for half in range(2):
                        rhs = e[:, N * half:N * half + N]
                        if g == 0:
                            c = 2 * k + half
                            for b in range(HB):
                                mm = nc.tensor.matmul(pf[b][:, 0:N], w1_sb[:, c, P * b:P * b + P], rhs,
                                                      start=(c == 0), stop=(c == 23))
                        else:
                            hb = 2 * (g - 1) + half
                            first, last = g == 1 and k == 0 and half == 0, g == 2 and k == 15 and half == 1
                            for m in range(2):
                                mm = nc.tensor.matmul(pf[m][0:HC, 0:N], w2_sb[:, k, hb, HC * m:HC * m + HC], rhs,
                                                      start=first, stop=last)
                    mm.then_inc(s_slot, 1)
                elif kind == "res":
                    t = step[1]
                    eng.wait_ge(s_ffn, i * 2 + 2)
                    eng.wait_ge(s_hid, i * HB + HB)
                    if t == 2:
                        eng.wait_ge(s_res, i * NT + 1)
                    for c in range(2):
                        mm = nc.tensor.transpose(pf[2 + t % 2][0:TT, HC * c:HC * c + HC], yf[:, c, cols(t)],
                                                 ident[0:HC, 0:HC])
                    mm.then_inc(s_rT, 1)

            eng.wait_ge(s_const, 16 * 9)
            eng.wait_ge(s_wffn, 32)
            run(eng, front, back)

        @block.scalar
        def _(eng):
            act = nc.scalar.activation

            def front(i, step):
                kind, t = step
                if kind in ("yT", "v", "oT", "zT") or (kind == "qk" and t < 2):
                    j = JOB[step]
                    src = ring[j % 3]
                    eng.wait_ge(s_job, i * len(JOBS) + j + 1)
                if kind == "yT":
                    act(yT[:, :, cols(t)], src[0:HC, 0:2 * TT].rearrange("p (c n) -> p c n", c=2),
                        ACT.Copy).then_inc(s_evac["act"], 1)
                elif kind == "qk" and t < 2:
                    act(q[:, t, 0, :], src[0:HC, 0:N], ACT.Copy, scale=small[0:HC, 4:5]).then_inc(s_half, 1)
                    act(q[:, t, 1, :], src[0:HC, 0:N], ACT.Copy, scale=small[0:HC, 5:6]).then_inc(s_evac["act"], 1)
                elif kind == "v":
                    act(v[:, t, :, 0:D], src[0:TT, 0:C].rearrange("p (h d) -> p h d", d=D),
                        ACT.Copy).then_inc(s_evac["act"], 1)
                elif kind == "oT":
                    if t < 2:
                        act(oT[:, :, SKIP + P * t:SKIP + P * t + P],
                            src[0:HC, 0:2 * P].rearrange("p (c n) -> p c n", c=2), ACT.Copy).then_inc(s_evac["act"], 1)
                    else:
                        act(oT[:, :, 0:SKIP], src[0:HC, 0:2 * P].rearrange("p (c n) -> p c n", c=2)[:, :, 0:SKIP],
                            ACT.Copy).then_inc(s_evac["act"], 1)
                elif kind == "zT":
                    if t == 0:
                        wait(eng, s_cd, (i - 1) * 3 * N_CD + 3)
                    act(x1[:, :].rearrange("p (c n) -> p c n", c=2)[:, :, cols(t)],
                        src[:, 0:2 * TT].rearrange("p (c n) -> p c n", c=2), ACT.Copy,
                        bias=XBIAS, scale=XSCALE).then_inc(s_evac["act"], 1)
                elif kind == "scores":
                    u = t
                    eng.wait_ge(s_max, i * ATT_TILES + u + 1)
                    if u >= S_BUF:
                        eng.wait_ge(s_ptr, i * ATT_TILES + u - S_BUF + 1)
                    act(probs[:, u % S_BUF, :], ps[u % 2][:, 0:N], ACT.Exp,
                        bias=nmax[:, u % S_BUF:u % S_BUF + 1]).then_inc(s_exp, 1)
                elif kind == "pT":
                    u = t
                    eng.wait_ge(s_ptr, i * ATT_TILES + u + 1)
                    if u >= 2:
                        eng.wait_ge(s_pv, i * ATT_TILES + u - 1)
                    act(pT[:, u % 2, :], pt[0:TT, 0:3 * P], ACT.Copy).then_inc(s_ptc, 1)

            def back(i, step):
                kind = step[0]
                if kind == "prep" and step[2][0] == "a":
                    g, o = step[1], int(step[2][1:])
                    base_d, base_a = (i * 3 + g) * N_CD, (i * 3 + g) * N_CA
                    s0, e1, e0, s1 = (val[:, g % 2, m, :] for m in range(4))
                    if o == 0:
                        eng.wait_ge(s_cd, base_d + 3)
                        act(ta[:, :], g_[:, :], ACT.Abs, scale=4.0).then_inc(s_ca, 1)
                    elif o == 1:
                        eng.wait_ge(s_ca, base_a + 1)
                        act(e0, ta[:, :], ACT.Copy, scale=-1.0, bias=1.0).then_inc(s_ca, 1)
                    elif o == 2:
                        act(s0, ta[:, :], ACT.Square, scale=-1.0, bias=1.0).then_inc(s_ca, 1)
                    elif o == 3:
                        act(ty[:, :], ta[:, :], ACT.Abs, scale=-1.0, bias=1.0).then_inc(s_ca, 1)
                    elif o == 4:
                        eng.wait_ge(s_cd, base_d + 5)
                        act(s1, e1, ACT.Square, scale=4.0).then_inc(s_ca, 1)
                elif kind == "hidden":
                    b = step[1]
                    if b == 0:
                        eng.wait_ge(s_slot, i * NSLOT + SLOTS[0])
                        eng.wait_ge(s_cd, i * 3 * N_CD + 3)
                    act(x2[:, b, :], pf[b][:, 0:N], ACT.Copy, scale=XSCALE / 6.0, bias=XBIAS).then_inc(s_hid, 1)
                elif kind == "ffn_out":
                    eng.wait_ge(s_slot, (i + 1) * NSLOT)
                    wait(eng, s_rT, i * NT)
                    for m in range(2):
                        act(yf[:, m, :], pf[m][0:HC, 0:N], ACT.Copy, scale=1.0 / 6.0).then_inc(s_ffn, 1)

            eng.wait_ge(s_const, 16 * 9)
            run(eng, front, back)

        @block.vector
        def _(eng):
            ve = nc.vector

            def front(i, step):
                kind, t = step
                if kind in ("tok", "proj") or (kind == "qk" and t >= 2):
                    j = JOB[step]
                    src = ring[j % 3]
                    eng.wait_ge(s_job, i * len(JOBS) + j + 1)
                if kind == "tok":
                    n = TT if t < 2 else N_IMG - 2 * TT
                    if t == 0:
                        wait(eng, s_keep, i)
                    ve.tensor_tensor(h_sb[0:n, t, :], src[0:n, 0:C], tokb_sb[0:n, :], ALU.add).then_inc(s_evac["dve"], 1)
                elif kind == "ln":
                    base = (i * 2 + t) * N_LN
                    if t == 0:
                        eng.wait_ge(s_txt, 16 * (i + 1))
                        wait_job(eng, i, JOB[("tok", NT - 1)])
                    else:
                        wait_job(eng, i, JOB[("proj", NT - 1)])
                    for m in range(NT):
                        ve.bn_stats(stats[:, m, :], h_sb[:, m, :]).then_inc(s_ln, 1)
                    for m in range(NT):
                        eng.wait_ge(s_ln, base + m + 1)
                        apart(eng)
                        ve.bn_aggr(mv[:, m, :], stats[:, m, :]).then_inc(s_ln, 1)
                    eng.wait_ge(s_rstd, i * 2 + t + 1)
                    if t == 1:
                        wait_job(eng, i, JOB[("yT", NT - 1)])
                    else:
                        if not first(i):
                            wait_job(eng, i - 1, JOB[("zT", NT - 1)])
                    for m in range(NT):
                        ve.tensor_scalar(z[:, m, 0:C], h_sb[:, m, :], mv[:, m, 0:1], rstd[:, m:m + 1],
                                         ALU.subtract, ALU.mult).then_inc(s_ln, 1)
                elif kind == "qk" and t >= 2:
                    half = t - 2
                    ve.tensor_scalar(kx[:, half, 0:SKIP], src[0:HC, 0:SKIP], rpe_sb[:, 7:8], None,
                                     ALU.add).then_inc(s_half, 1)
                    ve.tensor_scalar(kx[:, half, SKIP:N], src[0:HC, SKIP:N], rpe_sb[:, 3:4], None,
                                     ALU.add).then_inc(s_evac["dve"], 1)
                elif kind == "scores":
                    u = t
                    s = ps[u % 2]
                    eng.wait_ge(s_score, i * ATT_TILES + u + 1)
                    head, ti = att_tile(u)
                    base = i * N_FIX + fixes_before(u)
                    if ti is not None:
                        for n, w in enumerate((W2, W1, P)):
                            j0 = SKIP if ti == 0 else N - w
                            m = ident[:, :] if w == P else masks[:, ti, 0:W1] if w == W1 else masks[:, ti, W1:W1 + W2]
                            if n:
                                eng.wait_ge(s_fix, base + n)
                            ve.scalar_tensor_tensor(s[:, j0:j0 + w], m, s[:, N + 2 - n:N + 3 - n], s[:, j0:j0 + w],
                                                    ALU.mult, ALU.add).then_inc(s_fix, 1)
                        last = base + 3
                    else:
                        ve.tensor_scalar(s[:, SKIP:N], s[:, SKIP:N], s[:, N + 3:N + 4], None,
                                         ALU.add).then_inc(s_fix, 1)
                        last = base + 1
                    eng.wait_ge(s_fix, last)
                    if u >= S_BUF:
                        eng.wait_ge(s_exp, i * ATT_TILES + u - S_BUF + 1)
                    ve.tensor_reduce(nmax[:, u % S_BUF:u % S_BUF + 1], s[:, 0:N], AX_X, ALU.max,
                                     negate=True).then_inc(s_max, 1)
                elif kind == "pv" and t % 9 == 8:
                    g = t // 9
                    eng.wait_ge(s_pv, i * ATT_TILES + t + 1)
                    ve.tensor_copy(oC[:, 4 * g:4 * g + 4, :], o_C).then_inc(s_oc, 1)
                elif kind == "norm":
                    eng.wait_ge(s_pv, (i + 1) * ATT_TILES)
                    eng.wait_ge(s_oc, (i + 1) * 3)
                    ve.reciprocal(rs[:, :], o_AB[:, :, D]).then_inc(s_rs, 1)
                    ve.reciprocal(rsC[:, :], oC[:, :, D]).then_inc(s_rs, 1)
                    eng.wait_ge(s_rs, i * 2 + 1)
                    ve.tensor_tensor(oN[:, :, :], o_AB[:, :, 0:D], rs[:, :].unsqueeze(2).broadcast_to([P, 2 * H, D]),
                                     ALU.mult).then_inc(s_on, 1)
                    eng.wait_ge(s_rs, i * 2 + 2)
                    ve.tensor_tensor(oNC[:, :, :], oC[:, :, 0:D], rsC[:, :].unsqueeze(2).broadcast_to([32, H, D]),
                                     ALU.mult).then_inc(s_on, 1)
                elif kind == "proj":
                    if t == 0:
                        eng.wait_ge(s_hb, i + 1)
                    ve.tensor_tensor(h_sb[:, t, :], src[0:TT, 0:C], h_sb[:, t, :], ALU.add).then_inc(s_evac["dve"], 1)

            def back(i, step):
                kind = step[0]
                if kind == "prep" and step[2][0] == "d":
                    g, o = step[1], int(step[2][1:])
                    d, a = (i * 3 + g) * N_CD, (i * 3 + g) * N_CA
                    st = g % 2
                    x4 = x1[:, :] if g == 0 else x2[:, 2 * (g - 1):2 * g, :].rearrange("p a b -> p (a b)")
                    V = [val[:, st, m, :] for m in range(4)]
                    s0, e1, e0, s1 = V
                    I = [idx[:, st, m, :] for m in range(4)]
                    ts, stt, tt = ve.tensor_scalar, ve.scalar_tensor_tensor, ve.tensor_tensor
                    if o == 0:
                        if g == 0:
                            wait_job(eng, i, JOB[("zT", NT - 1)])
                        else:
                            eng.wait_ge(s_hid, i * HB + 2 * g)
                        op = ts(x4, x4, XLO, XHI, ALU.max, ALU.min)
                    elif o == 1:
                        eng.wait_ge(s_cd, d + 1)
                        op = ts(I[0], x4, MAGIC, MAGIC, ALU.add, ALU.subtract)
                    elif o == 2:
                        eng.wait_ge(s_cd, d + 2)
                        op = tt(g_[:, :], x4, I[0], ALU.subtract)
                    elif o == 3:
                        eng.wait_ge(s_cd, d + 3)
                        op = ts(e1, g_[:, :], -0.25, 0.25, ALU.max, ALU.min)
                    elif o == 4:
                        eng.wait_ge(s_cd, d + 4)
                        op = stt(e1, e1, 2.0, g_[:, :], ALU.mult, ALU.subtract)
                    elif o in (5, 6, 7):
                        m = o - 4
                        op = stt(I[m], g_[:, :], 0.25 * m - 0.5, I[0], ALU.is_ge, ALU.add)
                    elif o == 8:
                        eng.wait_ge(s_ca, a + 4)
                        op = stt(ty[:, :], ty[:, :], -1.5, s0, ALU.add, ALU.mult)
                    elif o == 9:
                        op = stt(e0, s0, -3.0, e0, ALU.add, ALU.mult)
                    elif o == 10:
                        eng.wait_ge(s_cd, d + 9)
                        op = ts(ta[:, :], ty[:, :], -2.0, 1.0, ALU.mult, ALU.add)
                    elif o == 11:
                        op = ts(ty[:, :], ty[:, :], 2.0, 2.0, ALU.mult, ALU.add)
                    elif o == 12:
                        eng.wait_ge(s_cd, d + 11)
                        op = tt(V[0], ta[:, :], e0, ALU.subtract)
                    elif o == 13:
                        op = tt(V[2], ta[:, :], e0, ALU.add)
                    elif o == 14:
                        eng.wait_ge(s_ca, a + 5)
                        op = stt(e1, s1, -3.0, e1, ALU.add, ALU.mult)
                    elif o == 15:
                        eng.wait_ge(s_cd, d + 15)
                        op = stt(V[3], e1, 4.0, ty[:, :], ALU.mult, ALU.add)
                    elif o == 16:
                        op = stt(V[1], e1, -4.0, ty[:, :], ALU.mult, ALU.add)
                    op.then_inc(s_cd, 1)
                elif kind == "slot":
                    _, g, k = step
                    n = SLOT0[g] + k
                    st = g % 2
                    if k == 0:
                        eng.wait_ge(s_cd, (i * 3 + g + 1) * N_CD)
                    wait(eng, s_slot, i * NSLOT + n - E_BUF + 1)
                    e = basis[:, n % E_BUF, :]
                    if g == 0:
                        for half in range(2):
                            c = 2 * k + half
                            o = e[:, N * half:N * half + N]
                            if c < NCP:
                                m, scal, x0 = c % 4, float(c // 4 + (c % 4 > 0)), 0
                            else:
                                kp = c - NCP
                                m, x0 = kp % 4, N
                                base = 2 * (kp // 4) + (m > 0)
                                scal = small[:, base:base + 1]
                            op = ve.scalar_tensor_tensor(o, idx[:, st, m, x0:x0 + N], scal, val[:, st, m, x0:x0 + N],
                                                         ALU.is_equal, ALU.mult)
                    else:
                        m = k % 4
                        op = ve.scalar_tensor_tensor(e, idx[:, st, m, :], float(k // 4 + (m > 0)), val[:, st, m, :],
                                                     ALU.is_equal, ALU.mult)
                    op.then_inc(s_basis, 1)
                elif kind == "res":
                    t = step[1]
                    eng.wait_ge(s_rT, i * NT + t + 1)
                    if t == 0:
                        wait(eng, s_out, 16 * i)
                        eng.wait_ge(s_keep, i + 1)
                    ve.tensor_tensor(o_sb[:, t, :], pf[2 + t % 2][0:TT, 0:C], hres[:, t, :],
                                     ALU.add).then_inc(s_res, 1)

            eng.wait_ge(s_const, 16 * 9)
            for half in range(2):
                for n, m in enumerate((0, 1, 2, 7)):
                    op = ve.tensor_scalar(kx[:, half, N + n:N + n + 1], rpe_sb[:, m:m + 1], rpe_sb[:, 3:4], None,
                                          ALU.subtract)
                    op.then_inc(s_ones, 1)
            ve.memset(v[:, :, :, D], 1.0).then_inc(s_ones, 1)
            run(eng, front, back)

        @block.gpsimd
        def _(eng):
            gp = nc.gpsimd

            def front(i, step):
                kind, t = step
                if kind == "ln":
                    base = (i * 2 + t) * N_LN
                    eng.wait_ge(s_ln, base + 6)
                    apart(eng)
                    gp.tensor_scalar(rstd[:, :], mv[:, :, 1], EPS, 1.0, ALU.add, ALU.mult).then_inc(s_var, 1)
                    eng.wait_ge(s_var, i * 2 + t + 1)
                    gp.tensor_tensor(rstd[:, :], rstd[:, :], small[0:TT, 6:7].broadcast_to([TT, NT]),
                                     ALU.pow).then_inc(s_rstd, 1)
                    if t == 0:
                        eng.wait_ge(s_ln, base + 9)
                        gp.tensor_tensor(h_sb[:, :, :], h_sb[:, :, :],
                                         projb_sb[:, :].unsqueeze(1).broadcast_to([TT, NT, C]),
                                         ALU.add).then_inc(s_hb, 1)
                    else:
                        for m in range(NT):
                            eng.wait_ge(s_ln, base + 6 + m + 1)
                            apart(eng)
                            gp.tensor_copy(z[:, m, C:256], z[:, m, P:C]).then_inc(s_dup, 1)
                elif kind == "keep":
                    wait(eng, s_res, i * NT)
                    apart(eng)
                    gp.tensor_copy(hres[:, :, :], h_sb[:, :, :]).then_inc(s_keep, 1)

            def back(i, step):
                pass

            eng.wait_ge(s_const, 16 * 9)
            run(eng, front, back)


def _bucket():
    alpha, beta, gamma = 1.9, 3.8, 15.2
    co = np.stack(np.meshgrid(np.arange(GRID), np.arange(GRID), indexing="ij"), -1).reshape(-1, 2).astype(np.float64)
    dis = np.round(np.sqrt(((co[:, None] - co[None]) ** 2).sum(-1)))
    far = np.minimum(np.round(alpha + np.log(np.maximum(dis, 1e-9) / alpha) / np.log(gamma / alpha) * (beta - alpha)),
                     beta).astype(np.int64)
    return np.where(dis <= alpha, np.round(dis).astype(np.int64), far)


def _constants():
    bucket = _bucket()
    masks = np.zeros((P, 2, W1 + W2), np.float32)
    for t in range(2):
        rows = bucket[P * t:P * t + P]
        for m, w, at in ((1, W1, 0), (2, W2, W1)):
            j0 = 0 if t == 0 else NG - w
            masks[:, t, at:at + w] = rows[:, j0:j0 + w] == m
            assert (rows == m).sum() == masks[:, t, at:at + w].sum()
    small = np.zeros((P, 8), np.float32)
    for n in range(4):
        small[:64, n], small[64:, n] = n, n + 1
    par = (np.arange(P) // D) % 2
    small[:, 4], small[:, 5] = QSCALE * (par == 0), QSCALE * (par == 1)
    small[:, 6] = -0.5
    return np.eye(P, dtype=np.float32), masks, small


def kernel(x, txt, L0_tok_W, L0_tok_b, L0_attn_qkv_w, L0_attn_proj_w, L0_attn_proj_b, L0_attn_rpe_w, L0_ffn_w1,
           L0_ffn_w2):
    import concourse.bacc as _bacc
    from concourse.bass_utils import run_bass_kernel_spmd as _run

    c = np.ascontiguousarray
    x, txt, tw, tb, qkv, pw, pb, rw, w1, w2 = (np.asarray(a) for a in (
        x, txt, L0_tok_W, L0_tok_b, L0_attn_qkv_w, L0_attn_proj_w, L0_attn_proj_b, L0_attn_rpe_w, L0_ffn_w1,
        L0_ffn_w2))
    xp = x.reshape(B, 3, 14, 16, 14, 16).transpose(0, 1, 2, 4, 3, 5).reshape(B, N_IMG, KP, P).transpose(0, 3, 2, 1)
    a = w1[:, 0:P, :].transpose(1, 2, 0)
    lo = [kp % 4 + 8 * (kp // 4) for kp in range(8)]
    t = w1[:, P:C, :].transpose(1, 2, 0)
    b = np.concatenate([t[:, lo, :], t[:, [k + 4 for k in lo], :]], axis=0)
    w1l = np.concatenate([a, b], axis=1)
    w2l = w2.transpose(1, 2, 0).reshape(HB, P, NCP, C).transpose(1, 2, 0, 3)
    ident, masks, small = _constants()
    arrays = {
        "xT": c(xp), "txt": c(txt), "tok_w": c(tw.T.reshape(KP, P, C).transpose(1, 0, 2)),
        "tok_b": c(np.broadcast_to(tb, (TT, C))), "wqkv": c(qkv.T.reshape(2, HC, 3 * C).transpose(1, 0, 2)),
        "wproj": c(pw.T.reshape(2, HC, C).transpose(1, 0, 2)), "proj_b": c(np.broadcast_to(pb, (TT, C))),
        "rpe": c(np.tile(rw, (HC // D, 1))), "w1": c(w1l), "w2": c(w2l), "ident_in": ident, "mask_in": masks,
        "small_in": small,
    }
    nc = _bacc.Bacc("TRN2", target_bir_lowering=False, num_devices=1)
    args = [nc.dram_tensor(n, v.shape, mybir.dt.from_np(v.dtype), kind="ExternalInput").ap() for n, v in arrays.items()]
    out = nc.dram_tensor("out", (B, N, C), F32, kind="ExternalOutput").ap()
    build(nc, *args, out)
    r = _run(nc, [arrays], core_ids=[0])
    return r.results[0]["out"]
```
